# Optimizing a Trainium2 kernel written in Bass

```python
import numpy as np
import jax
import jax.numpy as jnp

def _softmax(x, axis=-1):
    return jax.nn.softmax(x, axis=axis)
def _gelu(x):
    return jax.nn.gelu(x, approximate=True)
def _silu(x):
    return jax.nn.silu(x)
def _sigmoid(x):
    return jax.nn.sigmoid(x)
def _layernorm(x, axis=-1, eps=1e-5):
    m = jnp.mean(x, axis=axis, keepdims=True)
    v = jnp.var(x, axis=axis, keepdims=True)
    return (x - m) / jnp.sqrt(v + eps)
def _scatter_add(tgt, idx, src, axis=0):
    return tgt.at[idx].add(src)
def _segment_sum(src, seg, n):
    return jax.ops.segment_sum(src, seg, n)

kernel_name = 'mk_adj_resnorm_d1_adj_64_16c427'

def setup_inputs(seed: int = 0):
    np.random.seed(seed)
    _w = jnp.asarray
    def _rec_inputs():
        import jax
        import jax.numpy as jnp
        _gk = jax.random.key(seed)
        x = -9.806e-05 + 1 * jax.random.normal(jax.random.fold_in(_gk, 1), (8192, 64), jnp.float32)
        _a = jax.random.bernoulli(jax.random.fold_in(_gk, 2), 0.00195312, (8192, 8192))
        _a = jnp.logical_or(_a, jnp.swapaxes(_a, -1, -2))
        _a = jnp.logical_or(_a, jnp.eye(8192, dtype=bool))
        _af = _a.astype(jnp.float32)
        adj = _af
        return x, adj
    x, adj = _rec_inputs()
    def _L0_gnn_setup():
        import jax, jax.numpy as jnp
        import numpy as np
        N, D_IN, D_OUT = (8192, 64, 64)
        MAX_NEIGH = 100
        DECAY = 0.5
        key = jax.random.key(seed)
        k1, k2, k3, k4 = jax.random.split(key, 4)
        stdv = 1.0 / np.sqrt(D_OUT)
        inputs = {'input': jax.random.normal(k1, (N, D_IN), dtype=jnp.float32), 'adj': jax.random.randint(k2, (N, N), 0, 2).astype(jnp.float32), 'weight': jax.random.uniform(k3, (D_IN, D_OUT), minval=-stdv, maxval=stdv, dtype=jnp.float32), 'bias': jax.random.uniform(k4, (D_OUT,), minval=-stdv, maxval=stdv, dtype=jnp.float32)}
        return inputs
    _L0_gnn_all = _L0_gnn_setup()
    _L0_gnn_in = {k: v for k, v in _L0_gnn_all.items() if k in ('weight', 'bias', )}
    del _L0_gnn_all

    return {
        "x": x,
        "adj": adj,
        "L0_gnn_weight": _L0_gnn_in["weight"],
        "L0_gnn_bias": _L0_gnn_in["bias"],
    }

def reference(x, adj, L0_gnn_weight, L0_gnn_bias):
    import jax
    import jax.numpy as jnp
    def _L0_gnn_ref(input, adj, weight, bias):
        import jax, jax.numpy as jnp
        import numpy as np
        N, D_IN, D_OUT = (8192, 64, 64)
        MAX_NEIGH = 100
        DECAY = 0.5
        support = input @ weight
        mask = (adj != 0).astype(support.dtype)
        rank = jnp.cumsum(mask, axis=1)
        deg = rank[:, -1:]
        k = jnp.minimum(deg, float(MAX_NEIGH))
        pos = rank - (deg - k)
        w = mask * jnp.where(pos > 0, DECAY ** (k - pos), 0.0)
        out = w @ support + bias
        return out

    x = _layernorm(x + _L0_gnn_ref(x, adj, L0_gnn_weight, L0_gnn_bias), axis=-1)
    return x


_drawn_inputs = setup_inputs


def setup_inputs(seed=0):
    import zlib

    import numpy as np

    out = dict(_drawn_inputs(seed))
    spreads = {}
    factors = {}
    for name, (base, spread) in spreads.items():
        noise = np.random.default_rng([zlib.crc32(name.encode()), seed]).standard_normal(out[name].shape)
        drawn = base * np.exp(spread * noise) if base else spread * noise
        out[name] = jnp.asarray(drawn.astype(out[name].dtype))
    for name, factor in factors.items():
        out[name] = (out[name] * factor).astype(out[name].dtype)
    return out
```

```python
def bass_decayed_graph_layernorm(nc, x, x_columns, adj_blocks, weight, bias, out):
    from contextlib import ExitStack

    import concourse.bass as bass
    from concourse import mybir

    fp32, bf16, u16 = mybir.dt.float32, mybir.dt.bfloat16, mybir.dt.uint16
    ALU = mybir.AluOpType
    ACT = mybir.ActivationFunctionType
    AX = mybir.AxisListType

    P = 128
    N, D = x.shape
    BLOCKS = N // P
    SLABS, GROUPS, _, GROUP, ROWS = adj_blocks.shape
    CHAINS = 2
    RUN = ROWS // CHAINS
    TILES = ROWS // P
    RUN_TILES = RUN // P
    RING = 4
    PASS = GROUP * RING
    PASSES = BLOCKS // PASS
    MASKS = 8
    PARTS = 3
    PER_BANK = 2
    BANKS = TILES // PER_BANK
    MAX_NEIGH = 100
    OWN = 128
    SCALE = 2.0 ** (127 - MAX_NEIGH)
    EPS = 1e-5
    PREP = RUN // D
    PREPS = BLOCKS // PREP
    NORM_STEPS = 10

    with ExitStack() as ctx:
        def sb(name, shape, dt):
            return ctx.enter_context(nc.sbuf_tensor(name, shape, dt))

        def pb(name, shape, dt):
            return ctx.enter_context(nc.psum_tensor(name, shape, dt))

        def sem(name):
            return ctx.enter_context(nc.semaphore(name))

        adj_ring = [sb(f"adj_ring{r}", [P, GROUP, ROWS], fp32) for r in range(RING)]
        mask = [sb(f"mask{i}", [P, ROWS], bf16) for i in range(MASKS)]
        wts = [[sb(f"wts{c}_{i}", [P, RUN], bf16) for i in range(2)] for c in range(CHAINS)]
        x_cols = sb("x_cols", [D, N], fp32)
        w_sb = sb("w_sb", [D, D], fp32)
        sup_f = sb("sup_f", [P, 2, PREP * D], fp32)
        left_f = sb("left_f", [P, 2, PREP * D], fp32)
        support = sb("support", [P, BLOCKS, PARTS, D], bf16)
        after = sb("after", [P, P], bf16)
        rest = sb("rest", [P, P], bf16)
        zeros = sb("zeros", [P, RUN], bf16)
        ones = sb("ones", [P, RUN], bf16)
        seed = sb("seed", [P, P], bf16)
        x_bias = sb("x_bias", [P, BLOCKS, D], fp32)
        bias_sb = sb("bias_sb", [P, D], fp32)
        sums = sb("sums", [P, TILES, PARTS, D], fp32)
        y = sb("y", [P, TILES, D], fp32)
        y2 = sb("y2", [P, TILES, D], fp32)
        mean = sb("mean", [P, TILES], fp32)
        var = sb("var", [P, TILES], fp32)
        inv = sb("inv", [P, TILES], fp32)
        minus_half = sb("minus_half", [P, TILES], fp32)
        result = sb("result", [P, TILES, D], fp32)

        count = [pb(f"count{c}", [P, RUN], fp32) for c in range(CHAINS)]
        acc = [pb(f"acc{b}", [P, RUN], fp32) for b in range(BANKS)]
        spare = [pb(f"spare{b}", [P, RUN], fp32) for b in range(2)]
        prep_bank = spare + count + acc

        ones_made = sem("ones_made")
        tri_steps = sem("tri_steps")
        tri_made = sem("tri_made")
        w_loaded = sem("w_loaded")
        cols_loaded = sem("cols_loaded")
        bias_loaded = sem("bias_loaded")
        x_loaded = sem("x_loaded")
        sup_summed = sem("sup_summed")
        sup_copied = sem("sup_copied")
        sup_steps = sem("sup_steps")
        sup_split = sem("sup_split")
        adj_loaded = [sem(f"adj_loaded{r}") for r in range(RING)]
        mask_ready = sem("mask_ready")
        mask_used = sem("mask_used")
        counted = [sem(f"counted{c}") for c in range(CHAINS)]
        wts_ready = [sem(f"wts_ready{c}") for c in range(CHAINS)]
        slab_summed = sem("slab_summed")
        sums_copied = sem("sums_copied")
        norm_steps = sem("norm_steps")
        inverted = sem("inverted")
        stored = sem("stored")

        block = ctx.enter_context(nc.Block())

        @block.sync
        def _(sp):
            sp.dma_start(w_sb[:, :], weight).then_inc(w_loaded, 16)
            sp.dma_start(x_cols[:, :], x_columns).then_inc(cols_loaded, 16)

            def load(r, slab, group):
                return sp.dma_start(adj_ring[r][:, :, :],
                                    adj_blocks[bass.ds(slab, 1), bass.ds(group, 1), :, :, :]
                                    .rearrange("s g p b r -> (s g p) b r")).then_inc(adj_loaded[r], 16)

            def load_pass(slab, q):
                before = sp.snap((slab * PASSES + q) * PASS - PASS)
                for r in range(RING):
                    compared = sp.to_reg(before + (r + 1) * GROUP)
                    load(r, slab, q * RING + r).wait_op(mask_ready, compared, "sem-ge")

            for r in range(RING):
                load(r, 0, r)
            sp.dma_start(bias_sb[:, :], bias.rearrange("(a d) -> a d", a=1).broadcast_to([P, D]))\
              .then_inc(bias_loaded, 16)
            sp.dma_start(x_bias[:, :, :], x.rearrange("(t p) d -> p t d", p=P)).then_inc(x_loaded, 16)
            with sp.Fori(1, PASSES) as q:
                load_pass(0, q)
            with sp.Fori(1, SLABS) as slab:
                with sp.Fori(0, PASSES) as q:
                    load_pass(slab, q)

        @block.gpsimd
        def _(pool):
            pool.memset(zeros[:, :], 0.0).then_inc(ones_made, 1)
            pool.memset(ones[:, :], 1.0).then_inc(ones_made, 1)
            pool.memset(seed[:, :], (MAX_NEIGH - OWN) / P).then_inc(ones_made, 1)
            pool.memset(after[:, :], 0.0).then_inc(tri_steps, 1)
            pool.memset(rest[:, :], -1.0).then_inc(tri_steps, 1)
            pool.wait_ge(tri_steps, 2)
            pool.affine_select(out=after[:, :], in_=after[:, :], compare_op=ALU.is_ge, fill=-1.0,
                               base=0, pattern=[[1, P]], channel_multiplier=-1).then_inc(tri_steps, 1)
            pool.affine_select(out=rest[:, :], in_=rest[:, :], compare_op=ALU.is_ge, fill=0.0,
                               base=0, pattern=[[1, P]], channel_multiplier=-1).then_inc(tri_steps, 1)
            pool.wait_ge(tri_steps, 4)
            pool.affine_select(out=after[:, :], in_=after[:, :], compare_op=ALU.not_equal,
                               fill=float(OWN), base=0, pattern=[[-1, P]], channel_multiplier=1)\
                .then_inc(tri_made, 1)
            pool.affine_select(out=rest[:, :], in_=rest[:, :], compare_op=ALU.not_equal,
                               fill=-1.0 - OWN, base=0, pattern=[[-1, P]], channel_multiplier=1)\
                .then_inc(tri_made, 1)
            pool.memset(minus_half[:, :], -0.5).then_inc(tri_steps, 1)
            pool.wait_ge(tri_steps, 5)
            pool.wait_ge(bias_loaded, 16)
            pool.wait_ge(x_loaded, 16)
            pool.tensor_tensor(x_bias[:, :, :], x_bias[:, :, :],
                               bias_sb[:, :].rearrange("p (a d) -> p a d", a=1).broadcast_to([P, BLOCKS, D]),
                               ALU.add).then_inc(norm_steps, 1)

            out_tiles = out.rearrange("(s t p) d -> s p t d", p=P, t=TILES)
            with pool.Fori(0, SLABS) as slab:
                before = pool.snap(slab * NORM_STEPS + 1)
                pool.wait_ge(norm_steps, before + (NORM_STEPS - 1))
                pool.tensor_tensor(inv[:, :], var[:, :], minus_half[:, :], ALU.pow).then_inc(inverted, 1)
                pool.wait_ge(norm_steps, before + NORM_STEPS)
                pool.dma_start(out_tiles[bass.ds(slab, 1), :, :, :].rearrange("s p t d -> (s p) t d"),
                               result[:, :, :]).then_inc(stored, 16)
            pool.wait_ge(stored, 16 * SLABS)

        @block.scalar
        def _(act):
            for s in range(PREPS):
                act.wait_ge(sup_summed, s + 1)
                if s >= 2:
                    act.wait_ge(sup_split, s - 1)
                act.activation(sup_f[:, s % 2, :], prep_bank[s][:, :], ACT.Copy, scale=SCALE)\
                   .then_inc(sup_copied, 1)
                first = BLOCKS - (s + 1) * PREP
                act.activation(support[:, first:first + PREP, 0, :],
                               prep_bank[s][:, :].rearrange("p (t d) -> p t d", d=D), ACT.Copy, scale=SCALE)\
                   .then_inc(sup_copied, 1)

            with act.Fori(0, SLABS) as slab:
                with act.Fori(0, PASSES) as q:
                    done = act.snap((slab * PASSES + q) * PASS)
                    for k in range(PASS):
                        for c in range(CHAINS):
                            act.wait_ge(counted[c], done + (k + 1))
                            act.activation(wts[c][k % 2][:, :].bitcast(u16), count[c][:, :], ACT.Relu,
                                           scale=128.0).then_inc(wts_ready[c], 1)
                act.wait_ge(slab_summed, slab + 1)
                act.wait_ge(norm_steps, slab * NORM_STEPS + 1)
                for b in range(BANKS):
                    act.activation(sums[:, b * PER_BANK:(b + 1) * PER_BANK, :, :],
                                   acc[b][:, 0:PER_BANK * PARTS * D]
                                   .rearrange("p (t s d) -> p t s d", t=PER_BANK, s=PARTS),
                                   ACT.Copy).then_inc(sums_copied, 1)

        @block.vector
        def _(dve):
            def split(s):
                first = BLOCKS - (s + 1) * PREP
                tiles = support[:, first:first + PREP, :, :]
                f = sup_f[:, s % 2, :].rearrange("p (t d) -> p t d", d=D)
                left = left_f[:, s % 2, :].rearrange("p (t d) -> p t d", d=D)
                dve.wait_ge(sup_copied, 2 * s + 2)
                dve.tensor_tensor(left, f, tiles[:, :, 0, :], ALU.subtract).then_inc(sup_steps, 1)
                dve.wait_ge(sup_steps, 2 * s + 1)
                dve.tensor_copy(tiles[:, :, 1, :], left).then_inc(sup_steps, 1)
                dve.wait_ge(sup_steps, 2 * s + 2)
                dve.tensor_tensor(tiles[:, :, 2, :], left, tiles[:, :, 1, :], ALU.subtract)\
                   .then_inc(sup_split, 1)

            def compare(k):
                dve.tensor_scalar(mask[k % MASKS][:, :], adj_ring[k // GROUP][:, k % GROUP, :], 0.0, None,
                                  ALU.not_equal).then_inc(mask_ready, 1)

            def compare_pass(slab, q):
                n = dve.snap(slab * PASSES + q)
                used_before = dve.snap(n * PASS - MASKS)
                for k in range(PASS):
                    if k % GROUP == 0:
                        dve.wait_ge(adj_loaded[k // GROUP], (n + 1) * 16)
                    dve.wait_ge(mask_used, used_before + (k + 1))
                    compare(k)

            def norm(slab):
                before = dve.snap(slab * NORM_STEPS + 1)
                steps = [0]

                def step(instruction):
                    instruction.then_inc(norm_steps, 1)
                    steps[0] += 1
                    if steps[0] < NORM_STEPS:
                        dve.wait_ge(norm_steps, before + steps[0])

                def spread(a):
                    return a[:, :].rearrange("p (t a) -> p t a", a=1).broadcast_to([P, TILES, D])

                tt = dve.tensor_tensor
                dve.wait_ge(norm_steps, before)
                dve.wait_ge(sums_copied, (slab + 1) * BANKS)
                step(tt(y[:, :, :], sums[:, :, 2, :], sums[:, :, 1, :], ALU.add))
                step(tt(y[:, :, :], y[:, :, :], sums[:, :, 0, :], ALU.add))
                step(tt(y[:, :, :], y[:, :, :], x_bias[:, bass.ds(slab * TILES, TILES), :], ALU.add))
                step(dve.tensor_reduce(mean[:, :], y[:, :, :], AX.X, ALU.add))
                step(dve.tensor_scalar(mean[:, :], mean[:, :], 1.0 / D, None, ALU.mult))
                step(tt(y[:, :, :], y[:, :, :], spread(mean), ALU.subtract))
                step(tt(y2[:, :, :], y[:, :, :], y[:, :, :], ALU.mult))
                step(dve.tensor_reduce(var[:, :], y2[:, :, :], AX.X, ALU.add))
                step(dve.tensor_scalar(var[:, :], var[:, :], 1.0 / D, EPS, ALU.mult, ALU.add))
                dve.wait_ge(inverted, slab + 1)
                if not isinstance(slab, int) or slab > 0:
                    dve.wait_ge(stored, slab * 16)
                step(tt(result[:, :, :], y[:, :, :], spread(inv), ALU.mult))
                assert steps[0] == NORM_STEPS

            for k in range(PASS):
                if k % GROUP == 0:
                    dve.wait_ge(adj_loaded[k // GROUP], 16)
                if k >= MASKS:
                    dve.wait_ge(mask_used, k - MASKS + 1)
                compare(k)
                if k < PREPS:
                    split(k)
            with dve.Fori(1, PASSES) as q:
                compare_pass(0, q)
            compare_pass(1, 0)
            norm(0)
            with dve.Fori(1, PASSES) as q:
                compare_pass(1, q)
            with dve.Fori(2, SLABS) as slab:
                compare_pass(slab, 0)
                norm(slab - 1)
                with dve.Fori(1, PASSES) as q:
                    compare_pass(slab, q)
            norm(SLABS - 1)

        @block.tensor
        def _(pe):
            mm = nc.tensor.matmul
            pe.wait_ge(w_loaded, 16)
            pe.wait_ge(cols_loaded, 16)
            for s in range(PREPS):
                for t in range(PREP):
                    tile = BLOCKS - (s + 1) * PREP + t
                    last = mm(prep_bank[s][:, t * D:(t + 1) * D], x_cols[:, tile * P:(tile + 1) * P],
                              w_sb[:, :], start=True, stop=True)
                last.then_inc(sup_summed, 1)
            pe.wait_ge(ones_made, 3)
            pe.wait_ge(tri_made, 2)

            def start_slab(slab):
                if isinstance(slab, int):
                    pe.wait_ge(sup_copied, 2 * PREPS)
                for c in range(CHAINS):
                    last = mm(count[c][:, :], seed[:, :], ones[:, :], start=True, stop=True,
                              skip_group_check=True)
                if not isinstance(slab, int):
                    last.then_inc(slab_summed, 1)
                    pe.wait_ge(sums_copied, slab * BANKS)
                for b in range(BANKS):
                    mm(acc[b][:, :], zeros[:, 0:P], zeros[:, :], start=True, stop=True, skip_group_check=True)

            def one_pass(slab, q, first=False):
                done = pe.snap((slab * PASSES + q) * PASS)
                first_blk = pe.snap((BLOCKS - 1) - q * PASS)

                def count_after(c, k):
                    if c == 0:
                        pe.wait_ge(mask_ready, done + (k + 1))
                    mm(count[c][:, :], after[:, :], mask[k % MASKS][:, c * RUN:(c + 1) * RUN],
                       start=False, stop=True, skip_group_check=True).then_inc(counted[c], 1)

                def count_rest_and_add_up(c, k, blk):
                    pe.wait_ge(wts_ready[c], done + (k + 1))
                    last = mm(count[c][:, :], rest[:, :], mask[k % MASKS][:, c * RUN:(c + 1) * RUN],
                              start=False, stop=True, skip_group_check=True)
                    if c == CHAINS - 1:
                        last.then_inc(mask_used, 1)
                    if first and c == 0 and k % PREP == 0:
                        pe.wait_ge(sup_split, k // PREP + 1)
                    for t in range(RUN_TILES):
                        tile = c * RUN_TILES + t
                        at = tile % PER_BANK * PARTS * D
                        last = mm(acc[tile // PER_BANK][:, at:at + PARTS * D],
                                  wts[c][k % 2][:, t * P:(t + 1) * P],
                                  support[:, bass.ds(blk, 1), :, :].rearrange("p b s d -> p (b s d)"),
                                  start=False, stop=True, skip_group_check=True)
                    return last

                count_after(0, 0)
                for k in range(PASS):
                    blk = pe.snap(first_blk - k)
                    count_after(1, k)
                    count_rest_and_add_up(0, k, blk)
                    if k + 1 < PASS:
                        count_after(0, k + 1)
                    last = count_rest_and_add_up(1, k, blk)
                return last

            start_slab(0)
            one_pass(0, 0, first=True)
            pe.wait_ge(sup_split, PREPS)
            with pe.Fori(1, PASSES) as q:
                one_pass(0, q)
            with pe.Fori(1, SLABS) as slab:
                start_slab(slab)
                with pe.Fori(0, PASSES) as q:
                    one_pass(slab, q)
            mm(spare[0][:, 0:P], zeros[:, 0:P], zeros[:, 0:P], start=True, stop=True)\
                .then_inc(slab_summed, 1)


def kernel(**inputs):
    import concourse.bacc as bacc
    import numpy as np
    from concourse import mybir
    from concourse.bass_utils import run_bass_kernel_spmd

    P, GROUP, ROWS = 128, 4, 1024
    x, adj = np.asarray(inputs["x"]), np.asarray(inputs["adj"])
    n = x.shape[0]
    adj_blocks = adj.T.reshape(n // (P * GROUP), GROUP, P, n // ROWS, ROWS)[::-1, ::-1].transpose(3, 0, 2, 1, 4)
    laid_out = {
        "x": x,
        "x_columns": x.T,
        "adj_blocks": adj_blocks,
        "weight": np.asarray(inputs["L0_gnn_weight"]),
        "bias": np.asarray(inputs["L0_gnn_bias"]),
    }
    nc = bacc.Bacc("TRN2", target_bir_lowering=False, num_devices=1)
    arrays, args = {}, []
    for name, a in laid_out.items():
        a = np.ascontiguousarray(a)
        arrays[f"in_{name}"] = a
        args.append(nc.dram_tensor(f"in_{name}", a.shape, mybir.dt.from_np(a.dtype), kind="ExternalInput").ap())
    args.append(nc.dram_tensor("out_0", x.shape, mybir.dt.float32, kind="ExternalOutput").ap())
    bass_decayed_graph_layernorm(nc, *args)
    return run_bass_kernel_spmd(nc, [arrays], core_ids=[0]).results[0]["out_0"]
```

```python
def bass_decayed_graph_layernorm(nc, x, x_columns, adj_blocks, weight, bias, out):
    from contextlib import ExitStack

    import concourse.bass as bass
    from concourse import mybir

    fp32, bf16, u16 = mybir.dt.float32, mybir.dt.bfloat16, mybir.dt.uint16
    ALU = mybir.AluOpType
    ACT = mybir.ActivationFunctionType
    AX = mybir.AxisListType

    P = 128
    N, D = x.shape
    BLOCKS = N // P
    SLABS, GROUPS, _, GROUP, ROWS = adj_blocks.shape
    CHAINS = 2
    RUN = ROWS // CHAINS
    TILES = ROWS // P
    RUN_TILES = RUN // P
    RING = 4
    PASS = GROUP * RING
    PASSES = BLOCKS // PASS
    MASKS = 8
    PARTS = 3
    PER_BANK = 2
    BANKS = TILES // PER_BANK
    CHAIN_BANKS = BANKS // CHAINS
    USED = PER_BANK * PARTS * D
    MAX_NEIGH = 100
    OWN = 128
    SCALE = 2.0 ** (127 - MAX_NEIGH)
    EPS = 1e-5
    PREP = RUN // D
    PREPS = BLOCKS // PREP
    NORM_STEPS = 10

    with ExitStack() as ctx:
        def sb(name, shape, dt):
            return ctx.enter_context(nc.sbuf_tensor(name, shape, dt))

        def pb(name, shape, dt):
            return ctx.enter_context(nc.psum_tensor(name, shape, dt))

        def sem(name):
            return ctx.enter_context(nc.semaphore(name))

        adj_ring = [sb(f"adj_ring{r}", [P, GROUP, ROWS], fp32) for r in range(RING)]
        mask = [sb(f"mask{i}", [P, ROWS], bf16) for i in range(MASKS)]
        wts = [[sb(f"wts{c}_{i}", [P, RUN], bf16) for i in range(2)] for c in range(CHAINS)]
        x_cols = sb("x_cols", [D, N], fp32)
        w_sb = sb("w_sb", [D, D], fp32)
        sup_f = sb("sup_f", [P, 2, PREP * D], fp32)
        left_f = sb("left_f", [P, 2, PREP * D], fp32)
        support = sb("support", [P, BLOCKS, PARTS, D], bf16)
        after = sb("after", [P, P], bf16)
        rest = sb("rest", [P, P], bf16)
        zeros = sb("zeros", [P, RUN], bf16)
        ones = sb("ones", [P, RUN], bf16)
        seed = sb("seed", [P, P], bf16)
        x_bias = sb("x_bias", [P, BLOCKS, D], fp32)
        bias_sb = sb("bias_sb", [P, D], fp32)
        sums = sb("sums", [P, TILES, PARTS, D], fp32)
        y = sb("y", [P, TILES, D], fp32)
        y2 = sb("y2", [P, TILES, D], fp32)
        mean = sb("mean", [P, TILES], fp32)
        var = sb("var", [P, TILES], fp32)
        inv = sb("inv", [P, TILES], fp32)
        minus_half = sb("minus_half", [P, TILES], fp32)
        result = sb("result", [P, TILES, D], fp32)

        count = [pb(f"count{c}", [P, RUN], fp32) for c in range(CHAINS)]
        acc = [pb(f"acc{b}", [P, RUN], fp32) for b in range(BANKS)]
        spare = [pb(f"spare{b}", [P, RUN], fp32) for b in range(2)]
        prep_bank = spare + count + acc

        def sums_of(b):
            return (sums[:, b * PER_BANK:(b + 1) * PER_BANK, :, :],
                    acc[b][:, 0:USED].rearrange("p (t s d) -> p t s d", t=PER_BANK, s=PARTS))

        ones_made = sem("ones_made")
        tri_steps = sem("tri_steps")
        tri_made = sem("tri_made")
        w_loaded = sem("w_loaded")
        cols_loaded = sem("cols_loaded")
        bias_loaded = sem("bias_loaded")
        x_loaded = sem("x_loaded")
        sup_summed = sem("sup_summed")
        sup_copied = sem("sup_copied")
        sup_steps = sem("sup_steps")
        sup_split = sem("sup_split")
        adj_loaded = [sem(f"adj_loaded{r}") for r in range(RING)]
        mask_ready = sem("mask_ready")
        mask_used = sem("mask_used")
        counted = [sem(f"counted{c}") for c in range(CHAINS)]
        wts_ready = [sem(f"wts_ready{c}") for c in range(CHAINS)]
        summed = [sem(f"summed{c}") for c in range(CHAINS)]
        sums_copied = [sem(f"sums_copied{c}") for c in range(CHAINS)]
        norm_steps = sem("norm_steps")
        inverted = sem("inverted")
        stored = sem("stored")

        block = ctx.enter_context(nc.Block())

        @block.sync
        def _(sp):
            sp.dma_start(w_sb[:, :], weight).then_inc(w_loaded, 16)
            sp.dma_start(x_cols[:, :], x_columns).then_inc(cols_loaded, 16)

            def load(r, slab, group):
                return sp.dma_start(adj_ring[r][:, :, :],
                                    adj_blocks[bass.ds(slab, 1), bass.ds(group, 1), :, :, :]
                                    .rearrange("s g p b r -> (s g p) b r")).then_inc(adj_loaded[r], 16)

            def load_pass(slab, q):
                before = sp.snap((slab * PASSES + q) * PASS - PASS)
                for r in range(RING):
                    compared = sp.to_reg(before + (r + 1) * GROUP)
                    load(r, slab, q * RING + r).wait_op(mask_ready, compared, "sem-ge")

            for r in range(RING):
                load(r, 0, r)
            sp.dma_start(bias_sb[:, :], bias.rearrange("(a d) -> a d", a=1).broadcast_to([P, D]))\
              .then_inc(bias_loaded, 16)
            sp.dma_start(x_bias[:, :, :], x.rearrange("(t p) d -> p t d", p=P)).then_inc(x_loaded, 16)
            with sp.Fori(1, PASSES) as q:
                load_pass(0, q)
            with sp.Fori(1, SLABS) as slab:
                with sp.Fori(0, PASSES) as q:
                    load_pass(slab, q)

        @block.gpsimd
        def _(pool):
            pool.memset(zeros[:, :], 0.0).then_inc(ones_made, 1)
            pool.memset(ones[:, :], 1.0).then_inc(ones_made, 1)
            pool.memset(seed[:, :], (MAX_NEIGH - OWN) / P).then_inc(ones_made, 1)
            pool.memset(after[:, :], 0.0).then_inc(tri_steps, 1)
            pool.memset(rest[:, :], -1.0).then_inc(tri_steps, 1)
            pool.wait_ge(tri_steps, 2)
            pool.affine_select(out=after[:, :], in_=after[:, :], compare_op=ALU.is_ge, fill=-1.0,
                               base=0, pattern=[[1, P]], channel_multiplier=-1).then_inc(tri_steps, 1)
            pool.affine_select(out=rest[:, :], in_=rest[:, :], compare_op=ALU.is_ge, fill=0.0,
                               base=0, pattern=[[1, P]], channel_multiplier=-1).then_inc(tri_steps, 1)
            pool.wait_ge(tri_steps, 4)
            pool.affine_select(out=after[:, :], in_=after[:, :], compare_op=ALU.not_equal,
                               fill=float(OWN), base=0, pattern=[[-1, P]], channel_multiplier=1)\
                .then_inc(tri_made, 1)
            pool.affine_select(out=rest[:, :], in_=rest[:, :], compare_op=ALU.not_equal,
                               fill=-1.0 - OWN, base=0, pattern=[[-1, P]], channel_multiplier=1)\
                .then_inc(tri_made, 1)
            pool.memset(minus_half[:, :], -0.5).then_inc(tri_steps, 1)
            pool.wait_ge(tri_steps, 5)
            pool.wait_ge(bias_loaded, 16)
            pool.wait_ge(x_loaded, 16)
            pool.tensor_tensor(x_bias[:, :, :], x_bias[:, :, :],
                               bias_sb[:, :].rearrange("p (a d) -> p a d", a=1).broadcast_to([P, BLOCKS, D]),
                               ALU.add).then_inc(norm_steps, 1)

            out_tiles = out.rearrange("(s t p) d -> s p t d", p=P, t=TILES)
            with pool.Fori(0, SLABS) as slab:
                before = pool.snap(slab * NORM_STEPS + 1)
                pool.wait_ge(norm_steps, before + (NORM_STEPS - 1))
                pool.tensor_tensor(inv[:, :], var[:, :], minus_half[:, :], ALU.pow).then_inc(inverted, 1)
                pool.wait_ge(norm_steps, before + NORM_STEPS)
                pool.dma_start(out_tiles[bass.ds(slab, 1), :, :, :].rearrange("s p t d -> (s p) t d"),
                               result[:, :, :]).then_inc(stored, 16)
            pool.wait_ge(stored, 16 * SLABS)

        @block.scalar
        def _(act):
            for s in range(PREPS):
                act.wait_ge(sup_summed, s + 1)
                if s >= 2:
                    act.wait_ge(sup_split, s - 1)
                act.activation(sup_f[:, s % 2, :], prep_bank[s][:, :], ACT.Copy, scale=SCALE)\
                   .then_inc(sup_copied, 1)
                first = BLOCKS - (s + 1) * PREP
                act.activation(support[:, first:first + PREP, 0, :],
                               prep_bank[s][:, :].rearrange("p (t d) -> p t d", d=D), ACT.Copy, scale=SCALE)\
                   .then_inc(sup_copied, 1)

            with act.Fori(0, SLABS) as slab:
                with act.Fori(0, PASSES) as q:
                    done = act.snap((slab * PASSES + q) * PASS)
                    for k in range(PASS):
                        for c in range(CHAINS):
                            act.wait_ge(counted[c], done + (k + 1))
                            act.activation(wts[c][k % 2][:, :].bitcast(u16), count[c][:, :], ACT.Relu,
                                           scale=128.0).then_inc(wts_ready[c], 1)
                act.wait_ge(summed[0], slab + 1)
                act.wait_ge(norm_steps, slab * NORM_STEPS + 1)
                for b in range(CHAIN_BANKS):
                    act.activation(*sums_of(b), ACT.Copy).then_inc(sums_copied[0], 1)

        @block.vector
        def _(dve):
            def split(s):
                first = BLOCKS - (s + 1) * PREP
                tiles = support[:, first:first + PREP, :, :]
                f = sup_f[:, s % 2, :].rearrange("p (t d) -> p t d", d=D)
                left = left_f[:, s % 2, :].rearrange("p (t d) -> p t d", d=D)
                dve.wait_ge(sup_copied, 2 * s + 2)
                dve.tensor_tensor(left, f, tiles[:, :, 0, :], ALU.subtract).then_inc(sup_steps, 1)
                dve.wait_ge(sup_steps, 2 * s + 1)
                dve.tensor_copy(tiles[:, :, 1, :], left).then_inc(sup_steps, 1)
                dve.wait_ge(sup_steps, 2 * s + 2)
                dve.tensor_tensor(tiles[:, :, 2, :], left, tiles[:, :, 1, :], ALU.subtract)\
                   .then_inc(sup_split, 1)

            def compare(k):
                dve.tensor_scalar(mask[k % MASKS][:, :], adj_ring[k // GROUP][:, k % GROUP, :], 0.0, None,
                                  ALU.not_equal).then_inc(mask_ready, 1)

            def copy_sums(slab):
                dve.wait_ge(summed[1], slab + 1)
                for b in range(CHAIN_BANKS, BANKS):
                    dve.tensor_copy(*sums_of(b)).then_inc(sums_copied[1], 1)

            def compare_pass(slab, q, sums_before=False):
                n = dve.snap(slab * PASSES + q)
                used_before = dve.snap(n * PASS - MASKS)
                for k in range(PASS):
                    if k % GROUP == 0:
                        dve.wait_ge(adj_loaded[k // GROUP], (n + 1) * 16)
                    dve.wait_ge(mask_used, used_before + (k + 1))
                    compare(k)
                    if sums_before and k == MASKS - 1:
                        copy_sums(slab - 1)

            def norm(slab):
                before = dve.snap(slab * NORM_STEPS + 1)
                steps = [0]

                def step(instruction):
                    instruction.then_inc(norm_steps, 1)
                    steps[0] += 1
                    if steps[0] < NORM_STEPS:
                        dve.wait_ge(norm_steps, before + steps[0])

                def spread(a):
                    return a[:, :].rearrange("p (t a) -> p t a", a=1).broadcast_to([P, TILES, D])

                tt = dve.tensor_tensor
                dve.wait_ge(norm_steps, before)
                for c in range(CHAINS):
                    dve.wait_ge(sums_copied[c], (slab + 1) * CHAIN_BANKS)
                step(tt(y[:, :, :], sums[:, :, 2, :], sums[:, :, 1, :], ALU.add))
                step(tt(y[:, :, :], y[:, :, :], sums[:, :, 0, :], ALU.add))
                step(tt(y[:, :, :], y[:, :, :], x_bias[:, bass.ds(slab * TILES, TILES), :], ALU.add))
                step(dve.tensor_reduce(mean[:, :], y[:, :, :], AX.X, ALU.add))
                step(dve.tensor_scalar(mean[:, :], mean[:, :], 1.0 / D, None, ALU.mult))
                step(tt(y[:, :, :], y[:, :, :], spread(mean), ALU.subtract))
                step(tt(y2[:, :, :], y[:, :, :], y[:, :, :], ALU.mult))
                step(dve.tensor_reduce(var[:, :], y2[:, :, :], AX.X, ALU.add))
                step(dve.tensor_scalar(var[:, :], var[:, :], 1.0 / D, EPS, ALU.mult, ALU.add))
                dve.wait_ge(inverted, slab + 1)
                if not isinstance(slab, int) or slab > 0:
                    dve.wait_ge(stored, slab * 16)
                step(tt(result[:, :, :], y[:, :, :], spread(inv), ALU.mult))
                assert steps[0] == NORM_STEPS

            for k in range(PASS):
                if k % GROUP == 0:
                    dve.wait_ge(adj_loaded[k // GROUP], 16)
                if k >= MASKS:
                    dve.wait_ge(mask_used, k - MASKS + 1)
                compare(k)
                if k < PREPS:
                    split(k)
            with dve.Fori(1, PASSES) as q:
                compare_pass(0, q)
            compare_pass(1, 0, sums_before=True)
            norm(0)
            with dve.Fori(1, PASSES) as q:
                compare_pass(1, q)
            with dve.Fori(2, SLABS) as slab:
                compare_pass(slab, 0, sums_before=True)
                norm(slab - 1)
                with dve.Fori(1, PASSES) as q:
                    compare_pass(slab, q)
            copy_sums(SLABS - 1)
            norm(SLABS - 1)

        @block.tensor
        def _(pe):
            mm = nc.tensor.matmul
            pe.wait_ge(w_loaded, 16)
            pe.wait_ge(cols_loaded, 16)
            for s in range(PREPS):
                for t in range(PREP):
                    tile = BLOCKS - (s + 1) * PREP + t
                    last = mm(prep_bank[s][:, t * D:(t + 1) * D], x_cols[:, tile * P:(tile + 1) * P],
                              w_sb[:, :], start=True, stop=True)
                last.then_inc(sup_summed, 1)
            pe.wait_ge(ones_made, 3)
            pe.wait_ge(tri_made, 2)

            def count_after(c, k, ready=None):
                if ready is not None:
                    pe.wait_ge(mask_ready, ready)
                mm(count[c][:, :], after[:, :], mask[k % MASKS][:, c * RUN:(c + 1) * RUN],
                   start=False, stop=True, skip_group_check=True).then_inc(counted[c], 1)

            def start_slab(slab):
                for c in range(CHAINS):
                    mm(count[c][:, :], seed[:, :], ones[:, :], start=True, stop=True, skip_group_check=True)
                    count_after(c, 0, slab * BLOCKS + 1 if c == 0 else None)
                for b in range(BANKS):
                    if not isinstance(slab, int) and b % CHAIN_BANKS == 0:
                        pe.wait_ge(sums_copied[b // CHAIN_BANKS], slab * CHAIN_BANKS)
                    mm(acc[b][:, 0:USED], zeros[:, 0:P], zeros[:, 0:USED], start=True, stop=True,
                       skip_group_check=True)

            def one_pass(slab, q, first=False, last=False):
                done = pe.snap((slab * PASSES + q) * PASS)
                first_blk = pe.snap((BLOCKS - 1) - q * PASS)
                for k in range(PASS):
                    blk = pe.snap(first_blk - k)
                    for c in range(CHAINS):
                        pe.wait_ge(wts_ready[c], done + (k + 1))
                        ends = last and k == PASS - 1
                        if not ends:
                            rows = slice(c * RUN, (c + 1) * RUN)
                            count_rest = mm(count[c][:, :], rest[:, :], mask[k % MASKS][:, rows],
                                            start=False, stop=True, skip_group_check=True)
                            if c == CHAINS - 1:
                                count_rest.then_inc(mask_used, 1)
                            count_after(c, (k + 1) % PASS, done + (k + 2) if c == 0 else None)
                        if first and c == 0 and k % PREP == 0:
                            pe.wait_ge(sup_split, k // PREP + 1)
                        for t in range(RUN_TILES):
                            tile = c * RUN_TILES + t
                            at = tile % PER_BANK * PARTS * D
                            add = mm(acc[tile // PER_BANK][:, at:at + PARTS * D],
                                     wts[c][k % 2][:, t * P:(t + 1) * P],
                                     support[:, bass.ds(blk, 1), :, :].rearrange("p b s d -> p (b s d)"),
                                     start=False, stop=True, skip_group_check=True)
                            if ends and c == CHAINS - 1 and t == 0:
                                add.then_inc(mask_used, 1)
                        if ends:
                            add.then_inc(summed[c], 1)

            pe.wait_ge(sup_copied, 2 * PREPS)
            start_slab(0)
            one_pass(0, 0, first=True)
            pe.wait_ge(sup_split, PREPS)
            with pe.Fori(1, PASSES - 1) as q:
                one_pass(0, q)
            one_pass(0, PASSES - 1, last=True)
            with pe.Fori(1, SLABS) as slab:
                start_slab(slab)
                with pe.Fori(0, PASSES - 1) as q:
                    one_pass(slab, q)
                one_pass(slab, PASSES - 1, last=True)


def kernel(**inputs):
    import concourse.bacc as bacc
    import numpy as np
    from concourse import mybir
    from concourse.bass_utils import run_bass_kernel_spmd

    P, GROUP, ROWS = 128, 4, 1024
    x, adj = np.asarray(inputs["x"]), np.asarray(inputs["adj"])
    n = x.shape[0]
    adj_blocks = adj.T.reshape(n // (P * GROUP), GROUP, P, n // ROWS, ROWS)[::-1, ::-1].transpose(3, 0, 2, 1, 4)
    laid_out = {
        "x": x,
        "x_columns": x.T,
        "adj_blocks": adj_blocks,
        "weight": np.asarray(inputs["L0_gnn_weight"]),
        "bias": np.asarray(inputs["L0_gnn_bias"]),
    }
    nc = bacc.Bacc("TRN2", target_bir_lowering=False, num_devices=1)
    arrays, args = {}, []
    for name, a in laid_out.items():
        a = np.ascontiguousarray(a)
        arrays[f"in_{name}"] = a
        args.append(nc.dram_tensor(f"in_{name}", a.shape, mybir.dt.from_np(a.dtype), kind="ExternalInput").ap())
    args.append(nc.dram_tensor("out_0", x.shape, mybir.dt.float32, kind="ExternalOutput").ap())
    bass_decayed_graph_layernorm(nc, *args)
    return run_bass_kernel_spmd(nc, [arrays], core_ids=[0]).results[0]["out_0"]
```

```python
def bass_decayed_graph_layernorm(nc, x_columns, adj_blocks, weight, bias, out):
    from contextlib import ExitStack

    import concourse.bass as bass
    from concourse import mybir

    fp32, bf16, fp16 = mybir.dt.float32, mybir.dt.bfloat16, mybir.dt.float16
    u16, i32 = mybir.dt.uint16, mybir.dt.int32
    ALU = mybir.AluOpType
    ACT = mybir.ActivationFunctionType
    AX = mybir.AxisListType

    P = 128
    D, N = x_columns.shape
    BLOCKS = N // P
    SLABS, GROUPS, _, GROUP, ROWS = adj_blocks.shape
    CHAINS = 2
    RUN = ROWS // CHAINS
    TILES = ROWS // P
    RUN_TILES = RUN // P
    RING = 4
    PASS = GROUP * RING
    PASSES = BLOCKS // PASS
    MASKS = PASS
    BY_BLOCKS = 2
    NORM_AT = 2
    PARTS = 2
    assert PARTS * D == P
    MAX_NEIGH = 100
    OWN = 128
    SMALL = 127 - MAX_NEIGH
    TOP = 14
    BIAS, MANTISSA = 127, 23
    EPS = 1e-5
    PREP = RUN // D
    PREPS = BLOCKS // PREP
    NORM_STEPS = 9
    VAR_STEP = 7

    with ExitStack() as ctx:
        def sb(name, shape, dt):
            return ctx.enter_context(nc.sbuf_tensor(name, shape, dt))

        def pb(name, shape, dt):
            return ctx.enter_context(nc.psum_tensor(name, shape, dt))

        def sem(name):
            return ctx.enter_context(nc.semaphore(name))

        adj_ring = [sb(f"adj_ring{r}", [P, GROUP, ROWS], fp32) for r in range(RING)]
        mask = [sb(f"mask{i}", [P, ROWS], bf16) for i in range(MASKS)]
        wts = [[sb(f"wts{c}_{i}", [P, RUN], bf16) for i in range(2)] for c in range(CHAINS)]
        x_cols = sb("x_cols", [D, N], fp32)
        w_sb = sb("w_sb", [D, D], fp32)
        sup_last = sb("sup_last", [P, PREP * D], fp32)
        largest = sb("largest", [P, PREPS], fp32)
        largest_row = sb("largest_row", [P, 1], fp32)
        exponent = sb("exponent", [1, 4], fp32)
        scales = sb("scales", [P, 2], fp32)
        ident = sb("ident", [P, P], fp32)
        ones_f = sb("ones_f", [1, P], fp32)
        support = sb("support", [P, BLOCKS, PARTS, D], fp16)
        after = sb("after", [P, P], bf16)
        rest = sb("rest", [P, P], bf16)
        zeros = sb("zeros", [P, RUN], bf16)
        ones = sb("ones", [P, RUN], bf16)
        seed = sb("seed", [P, P], bf16)
        bias_sb = sb("bias_sb", [P, 1], fp32)
        y = sb("y", [P, TILES, D], fp32)
        sums = [sb(f"sums{c}", [P, RUN], fp32) for c in range(CHAINS)]
        halves = sb("halves", [P, TILES, 6], fp32)
        moments = sb("moments", [P, TILES, 2], fp32)
        var = sb("var", [P, TILES], fp32)
        inv = sb("inv", [P, TILES], fp32)
        minus_half = sb("minus_half", [P, TILES], fp32)
        result = sb("result", [P, TILES, D], fp32)

        count = [pb(f"count{c}", [P, RUN], fp32) for c in range(CHAINS)]
        acc = [pb(f"acc{c}", [P, RUN], fp32) for c in range(CHAINS)]
        spare = [pb(f"spare{b}", [P, RUN], fp32) for b in range(8 - 2 * CHAINS)]
        prep_bank = count + acc + spare
        rows_turned = spare[:CHAINS]
        turned, spread_scales = count[0][0:1, 0:P], count[0][:, P:P + 2]

        def of_step(s, part):
            first = BLOCKS - (s + 1) * PREP
            return support[:, first:first + PREP, part, :]

        def upper(s):
            return of_step(s, 0)

        def unscaled(s):
            return (prep_bank[s] if s else sup_last)[:, :].rearrange("p (t d) -> p t d", d=D)

        ones_made = sem("ones_made")
        const_steps = sem("const_steps")
        consts_made = sem("consts_made")
        w_loaded = sem("w_loaded")
        cols_loaded = sem("cols_loaded")
        bias_loaded = sem("bias_loaded")
        turns_made = [sem(f"turns_made{c}") for c in range(CHAINS)]
        sup_summed = sem("sup_summed")
        largest_found = sem("largest_found")
        last_copied = sem("last_copied")
        scale_steps = sem("scale_steps")
        turned_made = sem("turned_made")
        scales_spread = sem("scales_spread")
        scales_made = sem("scales_made")
        sup_upper = sem("sup_upper")
        sup_lower = sem("sup_lower")
        adj_loaded = [sem(f"adj_loaded{r}") for r in range(RING)]
        block_loaded = [sem(f"block_loaded{k}") for k in range(PASS)]
        mask_ready = sem("mask_ready")
        mask_used = sem("mask_used")
        counted = [sem(f"counted{c}") for c in range(CHAINS)]
        wts_ready = [sem(f"wts_ready{c}") for c in range(CHAINS)]
        summed = [sem(f"summed{c}") for c in range(CHAINS)]
        sums_copied = [sem(f"sums_copied{c}") for c in range(CHAINS)]
        norm_steps = sem("norm_steps")
        inverted = sem("inverted")
        stored = sem("stored")
        last_stored = sem("last_stored")

        block = ctx.enter_context(nc.Block())

        @block.sync
        def _(sp):
            sp.dma_start(w_sb[:, :], weight).then_inc(w_loaded, 16)
            sp.dma_start(x_cols[:, :], x_columns).then_inc(cols_loaded, 16)

            def load(r, slab, group):
                return sp.dma_start(adj_ring[r][:, :, :],
                                    adj_blocks[bass.ds(slab, 1), bass.ds(group, 1), :, :, :]
                                    .rearrange("s g p b r -> (s g p) b r")).then_inc(adj_loaded[r], 16)

            def load_pass(slab, q):
                before = sp.snap((slab * PASSES + q) * PASS - PASS)
                for r in range(RING):
                    compared = sp.to_reg(before + (r + 1) * GROUP)
                    load(r, slab, q * RING + r).wait_op(mask_ready, compared, "sem-ge")

            def load_pass_by_blocks(slab, q):
                before = sp.snap((slab * PASSES + q) * PASS - PASS)
                for k in range(PASS):
                    compared = sp.to_reg(before + (k + 1))
                    sp.dma_start(adj_ring[k // GROUP][:, k % GROUP, :],
                                 adj_blocks[slab, bass.ds(q * RING + k // GROUP, 1), :, k % GROUP, :]
                                 .rearrange("g p r -> (g p) r"))\
                      .then_inc(block_loaded[k], 16).wait_op(mask_ready, compared, "sem-ge")

            for r in range(RING):
                load(r, 0, r)
            sp.dma_start(bias_sb[D:P, :], bias.rearrange("(d a) -> d a", a=1))\
              .then_inc(bias_loaded, 16)
            with sp.Fori(1, PASSES) as q:
                load_pass(0, q)
            with sp.Fori(1, SLABS - 1) as slab:
                with sp.Fori(0, PASSES) as q:
                    load_pass(slab, q)
            with sp.Fori(0, BY_BLOCKS) as q:
                load_pass(SLABS - 1, q)
            with sp.Fori(BY_BLOCKS, PASSES) as q:
                load_pass_by_blocks(SLABS - 1, q)
            sp.wait_ge(norm_steps, SLABS * NORM_STEPS)
            sp.dma_start(out[SLABS - 1, :, :, :], result[:, :, :]).then_inc(last_stored, 16)
            sp.wait_ge(last_stored, 16)

        @block.gpsimd
        def _(pool):
            pool.memset(zeros[:, :], 0.0).then_inc(ones_made, 1)
            pool.memset(ones[:, :], 1.0).then_inc(ones_made, 1)
            pool.memset(seed[:, :], (MAX_NEIGH - OWN) / P).then_inc(ones_made, 1)
            pool.memset(after[:, :], 0.0).then_inc(const_steps, 1)
            pool.memset(rest[:, :], -1.0).then_inc(const_steps, 1)
            pool.wait_ge(const_steps, 2)
            pool.affine_select(out=after[:, :], in_=after[:, :], compare_op=ALU.is_ge, fill=-1.0,
                               base=0, pattern=[[1, P]], channel_multiplier=-1).then_inc(const_steps, 1)
            pool.affine_select(out=rest[:, :], in_=rest[:, :], compare_op=ALU.is_ge, fill=0.0,
                               base=0, pattern=[[1, P]], channel_multiplier=-1).then_inc(const_steps, 1)
            pool.wait_ge(const_steps, 4)
            pool.affine_select(out=after[:, :], in_=after[:, :], compare_op=ALU.not_equal,
                               fill=float(OWN), base=0, pattern=[[-1, P]], channel_multiplier=1)\
                .then_inc(consts_made, 1)
            pool.affine_select(out=rest[:, :], in_=rest[:, :], compare_op=ALU.not_equal,
                               fill=-1.0 - OWN, base=0, pattern=[[-1, P]], channel_multiplier=1)\
                .then_inc(consts_made, 1)
            pool.memset(ones_f[:, :], 1.0).then_inc(consts_made, 1)
            pool.memset(bias_sb[0:D, :], 0.0).then_inc(consts_made, 1)
            pool.memset(ident[:, :], 0.0).then_inc(const_steps, 1)
            pool.memset(minus_half[:, :], -0.5).then_inc(const_steps, 1)
            pool.wait_ge(const_steps, 6)
            pool.affine_select(out=ident[:, :], in_=ident[:, :], compare_op=ALU.not_equal, fill=1.0,
                               base=0, pattern=[[-1, P]], channel_multiplier=1).then_inc(consts_made, 1)
            def invert(slab):
                pool.wait_ge(norm_steps, slab * NORM_STEPS + VAR_STEP)
                pool.tensor_tensor(inv[:, :], var[:, :], minus_half[:, :], ALU.pow).then_inc(inverted, 1)

            def store(slab):
                pool.wait_ge(norm_steps, slab * NORM_STEPS + NORM_STEPS)
                pool.dma_start(out[bass.ds(slab, 1), :, :, :].rearrange("s p t d -> (s p) t d"),
                               result[:, :, :]).then_inc(stored, 16)

            with pool.Fori(0, SLABS - 1) as slab:
                invert(slab)
                store(slab)
            invert(SLABS - 1)
            pool.wait_ge(stored, 16 * (SLABS - 1))

        @block.scalar
        def _(act):
            act.wait_ge(sup_summed, 1)
            act.activation(sup_last[:, :], prep_bank[0][:, :], ACT.Copy).then_inc(last_copied, 1)
            act.wait_ge(scales_made, 1)
            for s in range(PREPS):
                act.activation(upper(s), unscaled(s), ACT.Copy, scale=scales[:, 0:1]).then_inc(sup_upper, 1)

            def make_weights(slab):
                with act.Fori(0, PASSES) as q:
                    done = act.snap((slab * PASSES + q) * PASS)
                    for k in range(PASS):
                        for c in range(CHAINS):
                            act.wait_ge(counted[c], done + (k + 1))
                            act.activation(wts[c][k % 2][:, :].bitcast(u16), count[c][:, :], ACT.Relu,
                                           scale=128.0).then_inc(wts_ready[c], 1)

            def copy_sums(slab, of=slice(0, P)):
                for c in range(CHAINS):
                    act.wait_ge(summed[c], slab + 1)
                    if not isinstance(slab, int) or slab > 0:
                        act.wait_ge(turns_made[c], slab)
                    act.activation(sums[c][of, :], acc[c][of, :], ACT.Identity, bias=bias_sb[of, 0:1],
                                   scale=scales[of, 1:2]).then_inc(sums_copied[c], 1)

            make_weights(0)
            act.wait_ge(consts_made, 5)
            act.wait_ge(bias_loaded, 16)
            copy_sums(0)
            with act.Fori(1, SLABS - 1) as slab:
                make_weights(slab)
                copy_sums(slab)
            make_weights(SLABS - 1)
            copy_sums(SLABS - 1, of=slice(D, P))

        @block.vector
        def _(dve):
            def find_scales():
                for s in range(PREPS):
                    dve.wait_ge(sup_summed, s + 1)
                    if s == 0:
                        dve.wait_ge(last_copied, 1)
                    dve.tensor_reduce(largest[:, s:s + 1], unscaled(s), AX.XY, ALU.max,
                                      apply_absolute_value=True).then_inc(scale_steps, 1)
                    if s in (1, 3, 5, PREPS - 2):
                        compare_group(s // 2 if s % 2 else RING - 1)
                dve.wait_ge(scale_steps, PREPS)
                dve.tensor_reduce(largest_row[:, :], largest[:, :], AX.X, ALU.max).then_inc(largest_found, 1)
                dve.wait_ge(turned_made, 1)
                dve.tensor_reduce(exponent[:, 0:1], turned, AX.X, ALU.max).then_inc(scale_steps, 1)
                dve.wait_ge(scale_steps, PREPS + 1)
                bits = exponent[:, :].bitcast(i32)
                dve.tensor_scalar(bits[:, 1:2], bits[:, 0:1], 255 << MANTISSA, None, ALU.bitwise_and)\
                   .then_inc(scale_steps, 1)
                dve.wait_ge(scale_steps, PREPS + 2)
                least = TOP << MANTISSA
                dve.tensor_scalar(bits[:, 3:4], bits[:, 1:2], float(least), float((SMALL - TOP) << MANTISSA),
                                  ALU.max, ALU.add).then_inc(scale_steps, 1)
                dve.wait_ge(scale_steps, PREPS + 3)
                dve.tensor_scalar(bits[:, 2:3], bits[:, 3:4], -1.0,
                                  float((2 * BIAS + SMALL) << MANTISSA), ALU.mult, ALU.add)\
                   .then_inc(scale_steps, 1)
                dve.wait_ge(scales_spread, 1)
                dve.tensor_copy(scales[:, :], spread_scales).then_inc(scales_made, 1)

            def lower(s):
                dve.wait_ge(sup_upper, s + 1)
                dve.scalar_tensor_tensor(out=of_step(s, 1), in0=unscaled(s), scalar=scales[:, 0:1],
                                         in1=upper(s), op0=ALU.mult, op1=ALU.subtract)\
                   .then_inc(sup_lower, 1)

            def compare_group(g):
                dve.wait_ge(adj_loaded[g], 16)
                for k in range(g * GROUP, (g + 1) * GROUP):
                    compare(k)

            def compare(k):
                dve.tensor_scalar(mask[k % MASKS][:, :], adj_ring[k // GROUP][:, k % GROUP, :], 0.0, None,
                                  ALU.not_equal).then_inc(mask_ready, 1)

            def compare_pass(slab, q, norm_of=None, by_blocks=False):
                n = dve.snap(slab * PASSES + q)
                used_before = dve.snap(n * PASS - MASKS)
                for k in range(PASS):
                    if by_blocks:
                        dve.wait_ge(block_loaded[k], (q - BY_BLOCKS + 1) * 16)
                    elif k % GROUP == 0:
                        dve.wait_ge(adj_loaded[k // GROUP], (n + 1) * 16)
                    dve.wait_ge(mask_used, used_before + (k + 1))
                    normed = norm_of is not None and CHAINS < k <= NORM_STEPS
                    if normed:
                        norm_waits(norm_of, k)
                    compare(k)
                    if normed:
                        norm_step(norm_of, k)

            def add_x(slab, c):
                dve.wait_ge(sums_copied[c], slab + 1)
                dve.tensor_tensor(sums[c][0:D, :], sums[c][0:D, :],
                                  x_cols[:, bass.ds(slab * ROWS + c * RUN, RUN)], ALU.add)\
                   .then_inc(norm_steps, 1)

            def norm_waits(slab, number):
                if number <= 2 * CHAINS:
                    dve.wait_ge(turns_made[number - CHAINS - 1], slab + 1)
                else:
                    dve.wait_ge(norm_steps, slab * NORM_STEPS + (number - 1))
                if number == NORM_STEPS:
                    dve.wait_ge(inverted, slab + 1)
                    if not isinstance(slab, int) or slab > 0:
                        dve.wait_ge(stored, slab * 16)

            def norm_step(slab, number):
                def spread(a):
                    return a[:, :].rearrange("p (t a) -> p t a", a=1).broadcast_to([P, TILES, D])

                first = 1 + 2 * CHAINS
                tt = dve.tensor_tensor
                if number < first:
                    c = number - CHAINS - 1
                    now = dve.tensor_reduce(
                        y[:, c * RUN_TILES:(c + 1) * RUN_TILES, :],
                        rows_turned[c][:, :].rearrange("p (t s d) -> p t d s", s=PARTS, d=D), AX.X, ALU.add)
                elif number == first:
                    for t in range(TILES):
                        now = dve.bn_stats(halves[:, t, :], y[:, t, :])
                elif number == first + 1:
                    for t in range(TILES):
                        now = dve.bn_aggr(moments[:, t, :], halves[:, t, :])
                elif number == VAR_STEP:
                    now = dve.tensor_scalar(var[:, :], moments[:, :, 1], EPS, None, ALU.add)
                elif number == VAR_STEP + 1:
                    now = tt(y[:, :, :], y[:, :, :], moments[:, :, 0:1].broadcast_to([P, TILES, D]),
                             ALU.subtract)
                else:
                    now = tt(result[:, :, :], y[:, :, :], spread(inv), ALU.mult)
                now.then_inc(norm_steps, 1)

            find_scales()
            for s in range(PREPS):
                lower(s)
            with dve.Fori(1, PASSES) as q:
                compare_pass(0, q)

            def next_slab(slab, by_blocks=False):
                compare_pass(slab, 0)
                for c in range(CHAINS):
                    add_x(slab - 1, c)
                compare_pass(slab, 1)
                compare_pass(slab, NORM_AT, norm_of=slab - 1, by_blocks=by_blocks)
                with dve.Fori(NORM_AT + 1, PASSES) as q:
                    compare_pass(slab, q, by_blocks=by_blocks)

            next_slab(1)
            with dve.Fori(2, SLABS - 1) as slab:
                next_slab(slab)
            next_slab(SLABS - 1, by_blocks=True)
            for c in range(CHAINS):
                dve.wait_ge(summed[c], SLABS)
                dve.wait_ge(turns_made[c], SLABS - 1)
                first = (SLABS - 1) * ROWS + c * RUN
                dve.scalar_tensor_tensor(out=sums[c][0:D, :], in0=acc[c][0:D, :], scalar=scales[0:D, 1:2],
                                         in1=x_cols[:, first:first + RUN], op0=ALU.mult, op1=ALU.add)\
                   .then_inc(norm_steps, 1)
            for number in range(CHAINS + 1, NORM_STEPS + 1):
                norm_waits(SLABS - 1, number)
                norm_step(SLABS - 1, number)

        @block.tensor
        def _(pe):
            mm = nc.tensor.matmul
            pe.wait_ge(w_loaded, 16)
            pe.wait_ge(cols_loaded, 16)
            for s in range(PREPS):
                for t in range(PREP):
                    tile = BLOCKS - (s + 1) * PREP + t
                    last = mm(prep_bank[s][:, t * D:(t + 1) * D], x_cols[:, tile * P:(tile + 1) * P],
                              w_sb[:, :], start=True, stop=True)
                last.then_inc(sup_summed, 1)
            pe.wait_ge(ones_made, 3)
            pe.wait_ge(consts_made, 5)
            pe.wait_ge(largest_found, 1)
            nc.tensor.transpose(turned, largest_row[:, :], ident[:, :]).then_inc(turned_made, 1)
            pe.wait_ge(scale_steps, PREPS + 4)
            mm(spread_scales, ones_f[:, :], exponent[:, 2:4], start=True, stop=True)\
                .then_inc(scales_spread, 1)

            def count_after(c, k, ready=None):
                if ready is not None:
                    pe.wait_ge(mask_ready, ready)
                mm(count[c][:, :], after[:, :], mask[k % MASKS][:, c * RUN:(c + 1) * RUN],
                   start=False, stop=True, skip_group_check=True).then_inc(counted[c], 1)

            def start_slab(slab):
                if isinstance(slab, int):
                    pe.wait_ge(sup_lower, len(count + acc))
                for c in range(CHAINS):
                    mm(count[c][:, :], seed[:, :], ones[:, :], start=True, stop=True, skip_group_check=True)
                    count_after(c, 0, slab * BLOCKS + 1 if c == 0 else None)
                for c in range(CHAINS):
                    if not isinstance(slab, int):
                        pe.wait_ge(sums_copied[c], slab)
                    mm(acc[c][:, :], zeros[:, 0:P], zeros[:, :], start=True, stop=True,
                       skip_group_check=True)

            def turn_sums(c):
                for t in range(RUN_TILES):
                    turn = nc.tensor.transpose(rows_turned[c][:, t * P:(t + 1) * P],
                                               sums[c][:, t * P:(t + 1) * P], ident[:, :])
                turn.then_inc(turns_made[c], 1)

            def one_pass(slab, q, last=False, turn=False):
                done = pe.snap((slab * PASSES + q) * PASS)
                first_blk = pe.snap((BLOCKS - 1) - q * PASS)
                for k in range(PASS):
                    blk = pe.snap(first_blk - k)
                    for c in range(CHAINS):
                        if turn and k == 0 and c == 0:
                            pe.wait_ge(norm_steps, (slab - 1) * NORM_STEPS + CHAINS)
                        pe.wait_ge(wts_ready[c], done + (k + 1))
                        ends = last and k == PASS - 1
                        if not ends:
                            rows = slice(c * RUN, (c + 1) * RUN)
                            count_rest = mm(count[c][:, :], rest[:, :], mask[k % MASKS][:, rows],
                                            start=False, stop=True, skip_group_check=True)
                            if c == CHAINS - 1:
                                count_rest.then_inc(mask_used, 1)
                            count_after(c, (k + 1) % PASS, done + (k + 2) if c == 0 else None)
                        pieces = 2 if ends and c == CHAINS - 1 else 1
                        for h in range(pieces):
                            rows = slice(h * RUN // pieces, (h + 1) * RUN // pieces)
                            add = mm(acc[c][:, rows],
                                     support[:, bass.ds(blk, 1), :, :].rearrange("p b s d -> p (b s d)"),
                                     wts[c][k % 2][:, rows], start=False, stop=True,
                                     skip_group_check=True)
                            if h < pieces - 1:
                                add.then_inc(mask_used, 1)
                        if ends:
                            add.then_inc(summed[c], 1)
                        if turn and k == 0:
                            turn_sums(c)

            start_slab(0)
            pe.wait_ge(sup_lower, PREPS)
            with pe.Fori(0, PASSES - 1) as q:
                one_pass(0, q)
            one_pass(0, PASSES - 1, last=True)
            with pe.Fori(1, SLABS) as slab:
                start_slab(slab)
                one_pass(slab, 0)
                one_pass(slab, 1, turn=True)
                with pe.Fori(2, PASSES - 1) as q:
                    one_pass(slab, q)
                one_pass(slab, PASSES - 1, last=True)
            for c in range(CHAINS):
                pe.wait_ge(norm_steps, (SLABS - 1) * NORM_STEPS + c + 1)
                pe.wait_ge(sums_copied[c], SLABS)
                turn_sums(c)


def kernel(**inputs):
    import concourse.bacc as bacc
    import numpy as np
    from concourse import mybir
    from concourse.bass_utils import run_bass_kernel_spmd

    P, GROUP, ROWS = 128, 4, 1024
    x, adj = np.asarray(inputs["x"]), np.asarray(inputs["adj"])
    n = x.shape[0]
    adj_blocks = adj.T.reshape(n // (P * GROUP), GROUP, P, n // ROWS, ROWS)[::-1, ::-1].transpose(3, 0, 2, 1, 4)
    laid_out = {
        "x_columns": x.T,
        "adj_blocks": adj_blocks,
        "weight": np.asarray(inputs["L0_gnn_weight"]),
        "bias": np.asarray(inputs["L0_gnn_bias"]),
    }
    nc = bacc.Bacc("TRN2", target_bir_lowering=False, num_devices=1)
    arrays, args = {}, []
    for name, a in laid_out.items():
        a = np.ascontiguousarray(a)
        arrays[f"in_{name}"] = a
        args.append(nc.dram_tensor(f"in_{name}", a.shape, mybir.dt.from_np(a.dtype), kind="ExternalInput").ap())
    out_shape = (n // ROWS, P, ROWS // P, x.shape[1])
    args.append(nc.dram_tensor("out_0", out_shape, mybir.dt.float32, kind="ExternalOutput").ap())
    bass_decayed_graph_layernorm(nc, *args)
    out = run_bass_kernel_spmd(nc, [arrays], core_ids=[0]).results[0]["out_0"]
    return np.ascontiguousarray(out.transpose(0, 2, 1, 3)).reshape(x.shape)
```
